# Optimizing a Trainium2 kernel written in Bass

```python
import numpy as np
import jax
import jax.numpy as jnp

def _softmax(x, axis=-1):
    return jax.nn.softmax(x, axis=axis)

def _gelu(x):
    return jax.nn.gelu(x, approximate=True)

def _silu(x):
    return jax.nn.silu(x)

def _sigmoid(x):
    return jax.nn.sigmoid(x)

def _layernorm(x, axis=-1, eps=1e-05):
    m = jnp.mean(x, axis=axis, keepdims=True)
    v = jnp.var(x, axis=axis, keepdims=True)
    return (x - m) / jnp.sqrt(v + eps)

def _scatter_add(tgt, idx, src, axis=0):
    return tgt.at[idx].add(src)

def _segment_sum(src, seg, n):
    return jax.ops.segment_sum(src, seg, n)
kernel_name = 'mk_pixart_resid_d2_seqx_r4_d3378c'

def setup_inputs(seed: int=0):
    np.random.seed(seed)
    _w = jnp.asarray

    def _rec_inputs():
        import jax
        import jax.numpy as jnp
        _rk = jax.random.key(seed)
        x = 7.22e-05 + 1 * jax.random.normal(jax.random.fold_in(_rk, 1), (16, 112, 256), jnp.float32)
        _lenS = 112 - jax.random.randint(jax.random.fold_in(_rk, 7), (16,), 0, max(1, 112 // 4) + 1, jnp.int32)
        _lenS2 = 375 - jax.random.randint(jax.random.fold_in(_rk, 8), (16,), 0, max(1, 375 // 4) + 1, jnp.int32)
        _ctx_1024P = jax.random.normal(jax.random.fold_in(_rk, 11), (16, 16, 256), jnp.float32)
        _ctx_1024c = jax.random.dirichlet(jax.random.fold_in(_rk, 511), 0.3 * jnp.ones((16,), jnp.float32), (16, 375))
        _ctx_1024t = jnp.einsum('bsk,bkd->bsd', _ctx_1024c, _ctx_1024P)
        _ctx_1024t = _ctx_1024t * jax.lax.rsqrt(jnp.mean(jnp.square(_ctx_1024t)) + 1e-12) * 0.953939
        ctx_1024 = 4.13588e-05 + 0.999923 * (_ctx_1024t + 0.3 * jax.random.normal(jax.random.fold_in(_rk, 611), (16, 375, 256), jnp.float32))
        condB_tau = jax.random.uniform(jax.random.fold_in(_rk, 12), (16,), jnp.float32, 0.0, 1.45372)
        fside_BxS2_0 = 0.0088954 + 1.00633 * jax.random.normal(jax.random.fold_in(_rk, 13), (16, 375), jnp.float32)
        return (x, ctx_1024, condB_tau, fside_BxS2_0)
    x, ctx_1024, condB_tau, fside_BxS2_0 = _rec_inputs()

    def _L0_xcond_setup():
        import jax, jax.numpy as jnp
        import numpy as np
        D_MODEL = 256
        N_HEADS = 16
        key = jax.random.key(seed)
        ks = jax.random.split(key, 16)
        B, L, S, D = (4, 512, 512, D_MODEL)
        inp = {'q': jax.random.normal(ks[0], (B, L, D), jnp.float32), 'k': jax.random.normal(ks[1], (B, S, D), jnp.float32), 'v': jax.random.normal(ks[2], (B, S, D), jnp.float32), 'tau': jax.random.uniform(ks[3], (B, 1), jnp.float32, 0.5, 1.5), 'delta': jax.random.normal(ks[4], (B, S), jnp.float32)}
        s = 1.0 / np.sqrt(D)
        inp['Wq'] = jax.random.normal(ks[5], (D, D), jnp.float32) * s
        inp['bq'] = jnp.zeros((D,), jnp.float32)
        inp['Wk'] = jax.random.normal(ks[6], (D, D), jnp.float32) * s
        inp['bk'] = jnp.zeros((D,), jnp.float32)
        inp['Wv'] = jax.random.normal(ks[7], (D, D), jnp.float32) * s
        inp['bv'] = jnp.zeros((D,), jnp.float32)
        inp['Wo'] = jax.random.normal(ks[8], (D, D), jnp.float32) * s
        inp['bo'] = jnp.zeros((D,), jnp.float32)
        return inp
    _L0_xcond_all = _L0_xcond_setup()
    _L0_xcond_in = {k: v for k, v in _L0_xcond_all.items() if k in ('Wq', 'bq', 'Wk', 'bk', 'Wv', 'bv', 'Wo', 'bo')}
    del _L0_xcond_all

    def _L0_ffn_setup():
        import jax, jax.numpy as jnp
        import numpy as np
        H = 256
        I = 128
        E = 64
        G = 8
        TOPK_GROUP = 4
        K = 8
        I_SH = 256
        SCALE = 2.5

        def _route(x, router_w, e_bias):
            T = x.shape[0]
            scores = jax.nn.sigmoid(x.astype(jnp.float32) @ router_w.T.astype(jnp.float32))
            sfc = jax.lax.stop_gradient(scores) + e_bias[None, :]
            group_scores = jax.lax.top_k(sfc.reshape(T, G, E // G), 2)[0].sum(-1)
            _, gidx = jax.lax.top_k(group_scores, TOPK_GROUP)
            gmask = jax.nn.one_hot(gidx, G, dtype=sfc.dtype).sum(1)
            smask = jnp.repeat(gmask, E // G, axis=1)
            masked = jnp.where(smask > 0, sfc, 0.0)
            _, topk_idx = jax.lax.top_k(masked, K)
            w = jnp.take_along_axis(scores, topk_idx, axis=1)
            w = w / (w.sum(-1, keepdims=True) + 1e-20)
            return (topk_idx, w * SCALE)
        key = jax.random.key(seed)
        ks = jax.random.split(key, 9)
        s = 0.02
        return {'hidden_states': jax.random.normal(ks[0], (2, 256, H), jnp.float32), 'router_w': jax.random.normal(ks[1], (E, H), jnp.float32) * s, 'e_bias': jnp.zeros((E,), jnp.float32), 'Wg': jax.random.normal(ks[2], (E, H, I), jnp.float32) * s, 'Wu': jax.random.normal(ks[3], (E, H, I), jnp.float32) * s, 'Wd': jax.random.normal(ks[4], (E, I, H), jnp.float32) * s, 'SWg': jax.random.normal(ks[5], (H, I_SH), jnp.float32) * s, 'SWu': jax.random.normal(ks[6], (H, I_SH), jnp.float32) * s, 'SWd': jax.random.normal(ks[7], (I_SH, H), jnp.float32) * s}
    _L0_ffn_all = _L0_ffn_setup()
    _L0_ffn_in = {k: v for k, v in _L0_ffn_all.items() if k in ('router_w', 'e_bias', 'Wg', 'Wu', 'Wd', 'SWg', 'SWu', 'SWd')}
    del _L0_ffn_all

    def _L1_xcond_setup():
        import jax, jax.numpy as jnp
        import numpy as np
        B, S, D, H = (2, 512, 256, 16)
        DK = D // H

        def _split_heads(x):
            b, s, _ = x.shape
            return x.reshape(b, s, H, DK).transpose(0, 2, 1, 3)
        key = jax.random.key(seed)
        ks = jax.random.split(key, 14)
        inp = {'query': jax.random.normal(ks[0], (B, S, D), jnp.float32), 'key': jax.random.normal(ks[1], (B, S, D), jnp.float32), 'value': jax.random.normal(ks[2], (B, S, D), jnp.float32), 'tau': jax.random.uniform(ks[3], (B, 1), jnp.float32, 0.5, 1.5), 'delta': jax.random.normal(ks[4], (B, S), jnp.float32)}
        sc = 1.0 / np.sqrt(D)
        for i, name in enumerate(['q', 'k', 'v', 'o']):
            inp[f'W{name}'] = jax.random.normal(ks[5 + 2 * i], (D, D), jnp.float32) * sc
            inp[f'b{name}'] = jax.random.normal(ks[6 + 2 * i], (D,), jnp.float32) * 0.01
        return inp
    _L1_xcond_all = _L1_xcond_setup()
    _L1_xcond_in = {k: v for k, v in _L1_xcond_all.items() if k in ('Wq', 'bq', 'Wk', 'bk', 'Wv', 'bv', 'Wo', 'bo')}
    del _L1_xcond_all

    def _L1_ffn_setup():
        import jax, jax.numpy as jnp
        import numpy as np
        E = 8
        TOPK = 2

        def _moe_forward(x, Wg, W1, W2, W3):
            B, S, D = x.shape
            xt = x.reshape(-1, D)
            T = xt.shape[0]
            logits = xt @ Wg.T
            scores = jax.nn.softmax(logits, axis=-1)
            w, idx = jax.lax.top_k(scores, TOPK)
            w = w / (w.sum(axis=-1, keepdims=True) + 1e-20)
            cw = jnp.zeros((T, E), xt.dtype).at[jnp.arange(T)[:, None], idx].add(w)
            h = jax.nn.silu(jnp.einsum('td,ehd->teh', xt, W1)) * jnp.einsum('td,ehd->teh', xt, W3)
            out = jnp.einsum('teh,edh->ted', h, W2)
            y = jnp.einsum('te,ted->td', cw, out)
            return y.reshape(B, S, D)
        key = jax.random.key(seed)
        k0, k1, k2, k3, k4 = jax.random.split(key, 5)
        B, S, D, H = (1, 512, 256, 704)
        scale = 0.02
        x = jax.random.normal(k0, (B, S, D), jnp.float32)
        Wg = jax.random.normal(k1, (E, D), jnp.float32) * scale
        W1 = jax.random.normal(k2, (E, H, D), jnp.float32) * scale
        W2 = jax.random.normal(k3, (E, D, H), jnp.float32) * scale
        W3 = jax.random.normal(k4, (E, H, D), jnp.float32) * scale
        return {'x': x, 'Wg': Wg, 'W1': W1, 'W2': W2, 'W3': W3}
    _L1_ffn_all = _L1_ffn_setup()
    _L1_ffn_in = {k: v for k, v in _L1_ffn_all.items() if k in ('Wg', 'W1', 'W2', 'W3')}
    del _L1_ffn_all
    return {'x': x, 'ctx_1024': ctx_1024, 'condB_tau': condB_tau, 'fside_BxS2_0': fside_BxS2_0, 'L0_xcond_Wq': _L0_xcond_in['Wq'], 'L0_xcond_bq': _L0_xcond_in['bq'], 'L0_xcond_Wk': _L0_xcond_in['Wk'], 'L0_xcond_bk': _L0_xcond_in['bk'], 'L0_xcond_Wv': _L0_xcond_in['Wv'], 'L0_xcond_bv': _L0_xcond_in['bv'], 'L0_xcond_Wo': _L0_xcond_in['Wo'], 'L0_xcond_bo': _L0_xcond_in['bo'], 'L0_ffn_router_w': _L0_ffn_in['router_w'], 'L0_ffn_e_bias': _L0_ffn_in['e_bias'], 'L0_ffn_Wg': _L0_ffn_in['Wg'], 'L0_ffn_Wu': _L0_ffn_in['Wu'], 'L0_ffn_Wd': _L0_ffn_in['Wd'], 'L0_ffn_SWg': _L0_ffn_in['SWg'], 'L0_ffn_SWu': _L0_ffn_in['SWu'], 'L0_ffn_SWd': _L0_ffn_in['SWd'], 'L1_xcond_Wq': _L1_xcond_in['Wq'], 'L1_xcond_bq': _L1_xcond_in['bq'], 'L1_xcond_Wk': _L1_xcond_in['Wk'], 'L1_xcond_bk': _L1_xcond_in['bk'], 'L1_xcond_Wv': _L1_xcond_in['Wv'], 'L1_xcond_bv': _L1_xcond_in['bv'], 'L1_xcond_Wo': _L1_xcond_in['Wo'], 'L1_xcond_bo': _L1_xcond_in['bo'], 'L1_ffn_Wg': _L1_ffn_in['Wg'], 'L1_ffn_W1': _L1_ffn_in['W1'], 'L1_ffn_W2': _L1_ffn_in['W2'], 'L1_ffn_W3': _L1_ffn_in['W3']}

def reference(x, ctx_1024, condB_tau, fside_BxS2_0, L0_xcond_Wq, L0_xcond_bq, L0_xcond_Wk, L0_xcond_bk, L0_xcond_Wv, L0_xcond_bv, L0_xcond_Wo, L0_xcond_bo, L0_ffn_router_w, L0_ffn_e_bias, L0_ffn_Wg, L0_ffn_Wu, L0_ffn_Wd, L0_ffn_SWg, L0_ffn_SWu, L0_ffn_SWd, L1_xcond_Wq, L1_xcond_bq, L1_xcond_Wk, L1_xcond_bk, L1_xcond_Wv, L1_xcond_bv, L1_xcond_Wo, L1_xcond_bo, L1_ffn_Wg, L1_ffn_W1, L1_ffn_W2, L1_ffn_W3):
    import jax
    import jax.numpy as jnp

    def _L0_xcond_ref(q, k, v, tau, delta, Wq, bq, Wk, bk, Wv, bv, Wo, bo):
        import jax, jax.numpy as jnp
        import numpy as np
        D_MODEL = 256
        N_HEADS = 16
        B, L, D = q.shape
        S = k.shape[1]
        H = N_HEADS
        E = D // H
        qh = (q @ Wq.T + bq).reshape(B, L, H, E)
        kh = (k @ Wk.T + bk).reshape(B, S, H, E)
        vh = (v @ Wv.T + bv).reshape(B, S, H, E)
        scale = 1.0 / np.sqrt(E).astype(np.float32)
        scores = jnp.einsum('blhe,bshe->bhls', qh, kh)
        scores = scores * tau[:, None, None, :] + delta[:, None, None, :]
        a = jax.nn.softmax(scale * scores, axis=-1)
        out = jnp.einsum('bhls,bshd->blhd', a, vh).reshape(B, L, D)
        return out @ Wo.T + bo

    def _L0_ffn_ref(hidden_states, router_w, e_bias, Wg, Wu, Wd, SWg, SWu, SWd):
        import jax, jax.numpy as jnp
        import numpy as np
        H = 256
        I = 128
        E = 64
        G = 8
        TOPK_GROUP = 4
        K = 8
        I_SH = 256
        SCALE = 2.5

        def _route(x, router_w, e_bias):
            T = x.shape[0]
            scores = jax.nn.sigmoid(x.astype(jnp.float32) @ router_w.T.astype(jnp.float32))
            sfc = jax.lax.stop_gradient(scores) + e_bias[None, :]
            group_scores = jax.lax.top_k(sfc.reshape(T, G, E // G), 2)[0].sum(-1)
            _, gidx = jax.lax.top_k(group_scores, TOPK_GROUP)
            gmask = jax.nn.one_hot(gidx, G, dtype=sfc.dtype).sum(1)
            smask = jnp.repeat(gmask, E // G, axis=1)
            masked = jnp.where(smask > 0, sfc, 0.0)
            _, topk_idx = jax.lax.top_k(masked, K)
            w = jnp.take_along_axis(scores, topk_idx, axis=1)
            w = w / (w.sum(-1, keepdims=True) + 1e-20)
            return (topk_idx, w * SCALE)
        orig_shape = hidden_states.shape
        x = hidden_states.reshape(-1, orig_shape[-1])
        T = x.shape[0]
        topk_idx, topk_w = _route(x, router_w, e_bias)
        coef = jnp.zeros((T, E), topk_w.dtype).at[jnp.arange(T)[:, None], topk_idx].add(topk_w)
        g = jnp.einsum('th,ehi->tei', x, Wg)
        u = jnp.einsum('th,ehi->tei', x, Wu)
        h = jax.nn.silu(g) * u * coef[:, :, None]
        moe_out = jnp.einsum('tei,eih->th', h, Wd)
        shared = jax.nn.silu(x @ SWg) * (x @ SWu) @ SWd
        return (moe_out + shared).reshape(orig_shape)

    def _L1_xcond_ref(query, key, value, tau, delta, Wq, bq, Wk, bk, Wv, bv, Wo, bo):
        import jax, jax.numpy as jnp
        import numpy as np
        B, S, D, H = (2, 512, 256, 16)
        DK = D // H

        def _split_heads(x):
            b, s, _ = x.shape
            return x.reshape(b, s, H, DK).transpose(0, 2, 1, 3)
        q = _split_heads(query @ Wq.T + bq)
        k = _split_heads(key @ Wk.T + bk)
        v = _split_heads(value @ Wv.T + bv)
        scores = jnp.einsum('bhqd,bhkd->bhqk', q, k)
        scores = scores * tau[:, :, None, None] + delta[:, None, None, :]
        scores = scores / jnp.sqrt(jnp.asarray(DK, scores.dtype))
        p_attn = jax.nn.softmax(scores, axis=-1)
        x = jnp.einsum('bhqk,bhkd->bhqd', p_attn, v)
        x = x.transpose(0, 2, 1, 3).reshape(query.shape[0], -1, H * DK)
        return x @ Wo.T + bo

    def _L1_ffn_ref(x, Wg, W1, W2, W3):
        import jax, jax.numpy as jnp
        import numpy as np
        E = 8
        TOPK = 2

        def _moe_forward(x, Wg, W1, W2, W3):
            B, S, D = x.shape
            xt = x.reshape(-1, D)
            T = xt.shape[0]
            logits = xt @ Wg.T
            scores = jax.nn.softmax(logits, axis=-1)
            w, idx = jax.lax.top_k(scores, TOPK)
            w = w / (w.sum(axis=-1, keepdims=True) + 1e-20)
            cw = jnp.zeros((T, E), xt.dtype).at[jnp.arange(T)[:, None], idx].add(w)
            h = jax.nn.silu(jnp.einsum('td,ehd->teh', xt, W1)) * jnp.einsum('td,ehd->teh', xt, W3)
            out = jnp.einsum('teh,edh->ted', h, W2)
            y = jnp.einsum('te,ted->td', cw, out)
            return y.reshape(B, S, D)
        return _moe_forward(x, Wg, W1, W2, W3)
    x = x + _L0_xcond_ref(_layernorm(x, axis=-1), ctx_1024, ctx_1024, condB_tau[:, None], fside_BxS2_0, L0_xcond_Wq, L0_xcond_bq, L0_xcond_Wk, L0_xcond_bk, L0_xcond_Wv, L0_xcond_bv, L0_xcond_Wo, L0_xcond_bo)
    x = x + _L0_ffn_ref(_layernorm(x, axis=-1), L0_ffn_router_w, L0_ffn_e_bias, L0_ffn_Wg, L0_ffn_Wu, L0_ffn_Wd, L0_ffn_SWg, L0_ffn_SWu, L0_ffn_SWd)
    x = x + _L1_xcond_ref(_layernorm(x, axis=-1), ctx_1024, ctx_1024, condB_tau[:, None], fside_BxS2_0, L1_xcond_Wq, L1_xcond_bq, L1_xcond_Wk, L1_xcond_bk, L1_xcond_Wv, L1_xcond_bv, L1_xcond_Wo, L1_xcond_bo)
    x = x + _L1_ffn_ref(_layernorm(x, axis=-1), L1_ffn_Wg, L1_ffn_W1, L1_ffn_W2, L1_ffn_W3)
    return x

_drawn_inputs = setup_inputs


def setup_inputs(seed=0):
    import zlib

    import numpy as np

    out = dict(_drawn_inputs(seed))
    spreads = {'L0_xcond_bq': (0.0, 0.503),
     'L0_xcond_bk': (0.0, 2.0),
     'L0_xcond_bv': (0.0, 0.1),
     'L0_xcond_bo': (0.0, 0.1),
     'L0_ffn_e_bias': (0.0, 0.8)}
    factors = {'fside_BxS2_0': 3.031,
     'L0_ffn_router_w': 7.845,
     'L0_ffn_Wg': 6.592,
     'L0_ffn_Wu': 6.538,
     'L0_ffn_Wd': 6.521,
     'L0_ffn_SWg': 4.174,
     'L0_ffn_SWu': 4.108,
     'L0_ffn_SWd': 4.121,
     'L1_xcond_bq': 63.465,
     'L1_xcond_bk': 64.0,
     'L1_xcond_bv': 6.598,
     'L1_xcond_bo': 7.418,
     'L1_ffn_Wg': 4.037,
     'L1_ffn_W1': 3.575,
     'L1_ffn_W2': 3.537,
     'L1_ffn_W3': 3.548}
    for name, (base, spread) in spreads.items():
        noise = np.random.default_rng([zlib.crc32(name.encode()), seed]).standard_normal(out[name].shape)
        drawn = base * np.exp(spread * noise) if base else spread * noise
        out[name] = jnp.asarray(drawn.astype(out[name].dtype))
    for name, factor in factors.items():
        out[name] = (out[name] * factor).astype(out[name].dtype)
    return out
```

```python
from contextlib import ExitStack

import numpy as np
import concourse.bass as bass
import concourse.mybir as mybir

F32 = mybir.dt.float32
I32 = mybir.dt.int32
ALU = mybir.AluOpType
ACT = mybir.ActivationFunctionType
AX = mybir.AxisListType

P = 128
B, Q, S, D = 16, 112, 375, 256
KD = D // P
NH, DH = 16, 16
HPC = P // DH
ST, SP_ = 3, 125
TB = Q * B
EPS = 1e-5
NX = 4
BIG = 3.0e38


class Layer:

    def __init__(self, number, experts, chosen, inner, ring, unroll, all_used):
        self.number, self.E, self.K, self.I, self.ring, self.unroll, self.all_used = number, experts, chosen, inner, ring, unroll, all_used
        self.chunks = [min(P, inner - c) for c in range(0, inner, P)]
        self.region = P + TB
        tiles = (TB * chosen + experts * (P if all_used else P - 1)) // P
        self.tiles = -(-tiles // unroll) * unroll
        self.up = KD * inner
        self.cols = 2 * self.up + len(self.chunks) * D


L0 = Layer(0, 64, 8, 128, 8, 4, False)
L1 = Layer(1, 8, 2, 704, 2, 4, True)
LAYERS = (L0, L1)
TT = 256

C_ID, C_TRI, C_HEAD, C_LT, C_T, C_R0, C_R1 = 0, 128, 240, 248, 312, 314, 378
C_MH = 386
C_E = 387
C_END = 387 + 64


def constants():
    c = np.zeros((P, C_END), np.float32)
    p = np.arange(P)
    c[:, C_ID:C_ID + P] = np.eye(P)
    c[:, C_TRI:C_TRI + Q] = p[:, None] < np.arange(Q)[None]
    c[:, C_HEAD:C_HEAD + HPC] = (p[:, None] // DH) == np.arange(HPC)
    c[:, C_LT:C_LT + 64] = (np.arange(8)[None] < np.arange(8)[:, None]).reshape(1, 64)
    c[:, C_T] = p
    c[:, C_T + 1] = p + P
    c[:, C_R0:C_R0 + L0.E] = np.arange(L0.E) * L0.region + P + 1
    c[:, C_R1:C_R1 + L1.E] = np.arange(L1.E) * L1.region + P + 1
    c[:, C_MH] = -0.5
    c[:, C_E:C_E + 64] = np.arange(64)
    return c


def build(nc, a, out):
    ctx = ExitStack()

    def sb(name, shape, dt=F32):
        return ctx.enter_context(nc.sbuf_tensor(name, shape, dt))

    sems = {}

    def sem(name):
        if name not in sems:
            sems[name] = ctx.enter_context(nc.semaphore(name))
        return sems[name]

    with ctx:
        bank = [ctx.enter_context(nc.psum_tensor(f"bank{i}", [P, 512], F32)) for i in range(8)]
        con = sb("con", [P, C_END])
        ident = con[:, C_ID:C_ID + P]
        ones = sb("ones", [Q, P])
        resid = sb("resid", [Q, B, D])
        xn = sb("xn", [Q, D])
        xnT = sb("xnT", [P, KD, Q])
        qT = sb("qT", [P, KD, Q])
        qblk = sb("qblk", [P, 2, KD, HPC, Q])
        ctxT = sb("ctxT", [P, 2, KD, S])
        kT = sb("kT", [P, 2, KD, S])
        vv = sb("vv", [SP_, 2, ST, D])
        draw = sb("draw", [Q, 2, S])
        dl = sb("dl", [Q, 2, S])
        tau = sb("tau", [P, B])
        taun = sb("taun", [P, B])
        xs = sb("xs", [Q, NX, S])
        smin = sb("smin", [Q, NX])
        rs = sb("rs", [Q, 2, NH])
        rinv = sb("rinv", [Q, NH])
        pT = sb("pT", [SP_, 2, ST * Q])
        oT4 = sb("oT4", [P, 4 * Q])
        o2 = sb("o2", [Q, D])
        o2T = sb("o2T", [P, KD, Q])
        xn2 = sb("xn2", [Q, 2, D])
        xn2T = sb("xn2T", [P, KD, Q])
        kept = sb("kept", [P, 2 * 8 * D])
        xnTall = kept[:, 0:KD * TB].rearrange("p (k t) -> p k t", k=KD)
        yg = kept[0:Q, :].rearrange("p (u k d) -> p u k d", u=2, k=8)
        st6 = sb("st6", [Q, 6])
        mv = sb("mv", [Q, 2, 2])
        rstd = sb("rstd", [Q, 2])
        veps = sb("veps", [Q, 2])
        eti = sb("eti", [P, 2], I32)
        wq = [sb(f"wq{l}", [P, KD, D]) for l in range(2)]
        wk = [sb(f"wk{l}", [P, KD, D]) for l in range(2)]
        wv = [sb(f"wv{l}", [P, KD, D]) for l in range(2)]
        wo = [sb(f"wo{l}", [P, KD, D]) for l in range(2)]
        bqk = [sb(f"bqk{l}", [P, 2, KD]) for l in range(2)]
        bvo = [sb(f"bvo{l}", [Q, 2, D]) for l in range(2)]
        rw = [sb(f"rw{l}", [P, KD, L.E]) for l, L in enumerate(LAYERS)]
        ebias = sb("ebias", [Q, L0.E])
        swu = sb("swu", [P, 2, KD, D])
        swd = sb("swd", [P, KD, D])
        EM = L0.E
        sg = sb("sg", [Q, EM])
        sc = sb("sc", [Q, EM])
        sfc = sb("sfc", [Q, EM])
        g8 = sb("g8", [Q, 8, 8])
        gs = sb("gs", [Q, 8])
        cmpa = sb("cmpa", [Q, 8, 8])
        cmpb = sb("cmpb", [Q, 8, 8])
        rank8 = sb("rank8", [Q, 8])
        keep8 = sb("keep8", [Q, 8])
        msk = sb("msk", [Q, EM])
        m8 = sb("m8", [Q, 8])
        rep = sb("rep", [Q, EM])
        sel = sb("sel", [Q, EM])
        wsel = sb("wsel", [Q, EM])
        wsum = sb("wsum", [Q, 1])
        winv = sb("winv", [Q, 1])
        coef = sb("coef", [Q, EM])
        run = sb("run", [P, EM])
        key = sb("key", [Q, EM])
        keys = [sb(f"keys{l}", [Q, B, L.E]) for l, L in enumerate(LAYERS)]
        p8 = sb("p8", [Q, 8])
        idx = sb("idx", [Q, 2, 8], I32)
        eq = sb("eq", [Q, 8, EM])
        w8 = [sb(f"w8{l}", [Q, B, L.K]) for l, L in enumerate(LAYERS)]
        cnt = sb("cnt", [P, EM])
        ntile = sb("ntile", [P, EM])
        cumA = sb("cumA", [P, EM])
        cumB = sb("cumB", [P, EM])
        back = sb("back", [P, EM])
        kmax = sb("kmax", [Q, EM])
        le = sb("le", [P, EM])
        lt2 = sb("lt2", [P, EM])
        et = sb("et", [P, 2])
        et2 = sb("et2", [P, 2])
        ex2 = sb("ex2", [P, 2])
        use2 = sb("use2", [P, 2])
        act = sb("act", [P, EM])
        arank = sb("arank", [P, EM])
        cumt = sb("cumt", [P, EM])
        load2 = sb("load2", [P, 2])
        fix = sb("fix", [P, 2])
        tabc = sb("tabc", [P, 5, 2], I32)
        tabr = sb("tabr", [1, 5, TT], I32)
        yidx_all = sb("yidx_all", [Q, B, 8], I32)
        yidx = sb("yidx", [Q, 2, 8], I32)
        fin = sb("fin", [Q, 2, D])
        zrow = sb("zrow", [P, D])
        xb = sb("xb", [P, 4, D])
        xT = sb("xT", [P, 2, KD, P])
        sgate = sb("sgate", [P, 2, 448 * 2])
        hh = sb("hh", [P, 2, 448 * 2])
        hT = sb("hT", [P, 2, 6 * P])
        yb = sb("yb", [P, 4, D])
        ringbuf = sb("ringbuf", [P, max(L.ring * L.cols for L in LAYERS)])
        ring = [ringbuf[:, 0:L.ring * L.cols].rearrange("p (r c) -> p r c", r=L.ring) for L in LAYERS]
        xs_d = [nc.dram_tensor(f"xs_d{l}", [L.E * L.region + P, D], F32, kind="Internal").ap() for l, L in enumerate(LAYERS)]
        y_d = [nc.dram_tensor(f"y_d{l}", [L.tiles * P, D], F32, kind="Internal").ap() for l, L in enumerate(LAYERS)]
        tab_d = [nc.dram_tensor(f"tab_d{l}", [5, TT], I32, kind="Internal").ap() for l in range(2)]

        def at(t, i):
            return t[:, bass.ds(i, 1), :].rearrange("p o f -> p (o f)")

        def wait(eng, s, value):
            if not (isinstance(value, int) and value <= 0):
                eng.wait_ge(s, value)

        def hold(eng):
            eng.sem_inc(s_held["dve" if eng is nc.vector else "pool"], 1)

        JOBS = ("OT", "O2T", "OP", "XT", "Q", "XT2", "K0", "LG", "K1", "V01", "V2", "RK")
        mm = {j: sem(j + "_mm") for j in JOBS}
        ev = {j: sem(j + "_ev") for j in JOBS}
        s_con, s_x = sem("constants_in"), sem("first_x_in")
        s_wkv, s_wq, s_wts = ([sem(f"{n}{l}_in") for l in range(2)] for n in ("wkv", "wq", "rest"))
        s_swts = sem("shared_weights_in")
        s_ctx = [sem(f"ctx_in{u}") for u in range(2)]
        s_ms = sem("memset_done")
        s_taun, s_dl, s_qblk = sem("tau_scaled"), sem("delta_scaled"), sem("qblk_done")
        s_sc, s_ttr, s_exp, s_t, s_pv = sem("scores_mm"), sem("scores_shifted"), sem("exp_done"), sem("probs_T"), sem("pv_mm")
        s_tev = sem("probsT_ev")
        s_oev = sem("attn_out_ev")
        s_var, s_rstd = [sem("var_q"), sem("var_x")], [sem("rstd_q"), sem("rstd_x")]
        s_veps = [sem("veps_q"), sem("veps_x")]
        s_xn, s_xn2, s_idx = sem("xn_done"), sem("xn2_done"), sem("slots_done")
        s_lgx, s_pl, s_sel = sem("logit_exp"), sem("probs_l1"), sem("chosen")
        s_scat = [sem(f"scattered{u}") for u in range(2)]
        s_free = sem("scatter_buffers_free")
        s_xall = sem("xnT_kept")
        s_dv = sem("dve_chain")
        s_gat = [sem(f"gathered{u}") for u in range(2)]
        s_cmb = sem("combined")
        s_route = sem("route_tables")
        s_tabo, s_tabi = sem("table_out"), sem("table_in")
        s_yi = sem("yidx_copied")
        s_zero = sem("zeros_written")
        s_wl = [[sem(f"w{l}_in{s}") for s in range(L.ring)] for l, L in enumerate(LAYERS)]
        s_wr = [sem(f"experts{l}_ready") for l in range(2)]
        s_xl = [sem(f"xtile_in{u}") for u in range(4)]
        s_yst = [sem(f"ytile_out{u}") for u in range(4)]
        s_txt, s_txe, s_gu, s_sil, s_h, s_ht, s_hte, s_dn, s_ye = (sem(x) for x in (
            "xtile_T", "xtile_T_ev", "gate_up_mm", "silu_done", "h_done", "h_T", "h_T_ev", "down_mm", "y_ev"))
        s_sgu, s_ssil, s_sh, s_sdn, s_sev = (sem(x) for x in ("sh_up_mm", "sh_silu", "sh_h", "sh_down_mm", "sh_ev"))
        s_out = [sem(f"out_done{u}") for u in range(2)]
        s_held = {e: sem(f"held_{e}") for e in ("dve", "pool")}
        FREE_CREDIT, SH_CREDIT, SEV_CREDIT, SDN_CREDIT = 1, 2, 2, 1
        WKV_IN, WQ_IN, REST_IN = 3 * 16, 16, (6 * 16, 4 * 16)
        TABLES_READY, ROWS_READY = (1, 3), (2, 4)
        SP_ATTN, SP_TAB, SP_SHARED, SP_ROWS, SP_FIN = (0, 23), (18, 41), 19, 42, 46

        STEP = {"XT": 0, "Q": 2, "V2": 2, "RK": 4, "OT": 4, "O2T": 6, "OP": 8, "K1": 9, "K0": 10, "XT2": 12, "LG": 14, "V01": 14}
        ROW = {"XT": 1, "Q": 1, "K0": 1, "K1": 1, "V01": 1, "V2": 1, "OT": -1, "O2T": -1, "OP": -1, "XT2": -1, "LG": -1, "RK": -2}
        BANK_JOBS = (("Q", "OT", "OP", "K0", "S15", "V01"), ("XT", "V2", "RK", "O2T", "K1", "XT2", "LG"))
        AHEAD_S, AHEAD_X, AHEAD_E = 3, 2, 1

        def score_bank(h):
            return h % 3 if h < NH - 1 else 6

        def in_layer(b, offset):
            return not isinstance(b, int) or 0 <= b + offset < B

        def bodies(eng, L, body, first, last):
            base = B * L.number
            first()
            body(base, 0, 0)
            body(base + 1, 1, 1)
            with eng.Fori(0, (B - 4) // 2) as i:
                body(i * 2 + (base + 2), i * 2 + 2, 0)
                body(i * 2 + (base + 3), i * 2 + 3, 1)
            body(base + B - 2, B - 2, 0)
            body(base + B - 1, B - 1, 1)
            last()

        block = ctx.enter_context(nc.Block())

        @block.sync
        def _(sp):
            def load_ctx(b, u):
                sp.dma_start(ctxT[:, u].rearrange("p k s -> p (k s)"), a["ctxT"][bass.ds(b, 1)].rearrange("o p f -> (o p) f")).then_inc(s_ctx[u], 16)
                sp.dma_start(draw[:, u, :], a["delta"][bass.ds(b, 1), :].rearrange("o s -> (o s)").partition_broadcast(Q)).then_inc(s_ctx[u], 16)

            def load(s, l, *names):
                tensors = {"wq": wq, "wk": wk, "wv": wv, "wo": wo, "rw": rw, "bqk": bqk}
                for n in names:
                    if n in tensors:
                        sp.dma_start(tensors[n][l][:, :, :], a[f"{n}{l}"]).then_inc(s, 16)
                    else:
                        sp.dma_start(bvo[l][:, ("bv", "bo").index(n), :], a[f"{n}{l}"].partition_broadcast(Q)).then_inc(s, 16)

            sp.dma_start(resid[:, 0:2, :], a["x"][:, 0:2, :]).then_inc(s_x, 16)
            sp.dma_start(tau[:, :], a["tau"].partition_broadcast(P)).then_inc(s_con, 16)
            sp.dma_start(con[:, :], a["con"]).then_inc(s_con, 16)
            load_ctx(0, 0)
            load(s_wkv[0], 0, "wk", "bqk", "wv")
            load(s_wq[0], 0, "wq")
            load_ctx(1, 1)
            load(s_wts[0], 0, "wo", "rw", "bv", "bo")
            sp.dma_start(resid[:, 2:B, :], a["x"][:, 2:B, :]).then_inc(s_wts[0], 16)
            sp.dma_start(ebias[:, :], a["ebias"].partition_broadcast(Q)).then_inc(s_wts[0], 16)
            sp.dma_start(swu[:, :, :, :], a["swu"]).then_inc(s_swts, 16)
            sp.dma_start(swd[:, :, :], a["swd"]).then_inc(s_swts, 16)
            load(s_wkv[1], 1, "wk", "bqk", "wv")
            load(s_wq[1], 1, "wq")
            load(s_wts[1], 1, "wo", "rw", "bv", "bo")
            sp.wait_ge(s_ms, 4)
            for l, L in enumerate(LAYERS):
                sp.dma_start(xs_d[l][0:L.E * L.region, :].rearrange("(e r) d -> r e d", e=L.E)[0:P], zrow[:, :].unsqueeze(1).to_broadcast([P, L.E, D])).then_inc(s_zero, 16)
                sp.dma_start(xs_d[l][L.E * L.region:, :], zrow[:, :]).then_inc(s_zero, 16)

            def stream_ctx(L):
                base = B * L.number

                def step(n, b, u):
                    wait(sp, mm["V01"], n + 1)
                    wait(sp, s_dl, n + 1)
                    load_ctx(b + 2, u)
                with sp.Fori(0, (B - 2) // 2) as i:
                    step(i * 2 + base, i * 2, 0)
                    step(i * 2 + (base + 1), i * 2 + 1, 1)

            def tile_loads(L):
                l = L.number
                for u in range(2):
                    sp.wait_ge(s_scat[u], scat_count(l, B // 2))
                sp.wait_ge(s_route, TABLES_READY[l])
                sp.dma_start(tab_d[l].rearrange("k (c p) -> p k c", p=P), tabc[:, :, :], allow_slow_non_contiguous=True).then_inc(s_tabo, 16)
                sp.wait_ge(s_tabo, 16 * (l + 1))
                sp.dma_start(tabr[:, :, :], tab_d[l].rearrange("(o k) t -> o k t", o=1)).then_inc(s_tabi, 16)
                sp.wait_ge(s_tabi, 16 * (l + 1))
                sp.wait_ge(s_zero, 16 * 4)
                t0 = sum(M.tiles for M in LAYERS[:l])
                def load(t, u):
                    r = sp.value_load(tabr[0:1, 0, bass.ds(t, 1)], min_val=0, max_val=L.E * L.region)
                    need = sp.value_load(tabr[0:1, 2, bass.ds(t, 1)], min_val=1, max_val=L.E)
                    sp.wait_ge(s_wr[l], need)
                    sp.dma_start(xb[:, u, :], xs_d[l][bass.ds(r, P), :]).then_inc(s_xl[u], 16)
                if l:
                    sp.wait_ge(s_txt, t0)
                for u in range(4):
                    load(u, u)
                with sp.Fori(0, L.tiles // 4 - 1) as i:
                    for u in range(4):
                        sp.wait_ge(s_txt, i * 4 + (t0 + u + 1))
                        load(i * 4 + (4 + u), u)

            def scat_count(l, n):
                return 16 * (L0.K * (n if l == 0 else B // 2) + (L1.K * n if l else 0))

            stream_ctx(L0)
            tile_loads(L0)
            for b in range(2):
                sp.wait_ge(s_dl, B)
                sp.wait_ge(mm["V01"], B)
                load_ctx(b, b)
            stream_ctx(L1)
            tile_loads(L1)
            def store(b, u, n):
                sp.wait_ge(s_cmb, n)
                sp.dma_start(out[bass.ds(b, 1)].rearrange("o q d -> (o q) d"), fin[:, u, :]).then_inc(s_out[u], 16)
            with sp.Fori(0, B // 2) as i:
                store(i * 2, 0, i * 2 + (B + 1))
                store(i * 2 + 1, 1, i * 2 + (B + 2))
            for u in range(2):
                sp.wait_ge(s_out[u], 16 * (B // 2))

        @block.tensor
        def _(pe):
            M0, M1 = bank[6], bank[7]
            pe.wait_ge(s_con, 32)
            pe.wait_ge(s_ms, 4)

            def transposes(dst, src, rows, width):
                for k in range(width // P):
                    last = pe.transpose(dst[:, k * rows:(k + 1) * rows], src[:, k * P:(k + 1) * P], ident[0:rows, 0:rows])
                return last

            def project(dst, lhs, rhs):
                for k in range(KD):
                    last = pe.matmul(dst, lhs(k), rhs(k), start=(k == 0), stop=(k == KD - 1))
                return last

            def attention(L):
                l = L.number
                base = B * l

                def job(j, n, u, prev):
                    for s, v in prev:
                        wait(pe, s, v)
                    if j == "OT":
                        pe.wait_ge(s_oev, n + 1)
                        for g in range(4):
                            last = pe.transpose(M0[0:Q, g * P:(g + 1) * P], oT4[:, g * Q:(g + 1) * Q], ident)
                    elif j == "O2T":
                        pe.wait_ge(ev["OT"], n + 1)
                        last = transposes(M1, o2, Q, D)
                    elif j == "OP":
                        pe.wait_ge(ev["O2T"], n + 1)
                        last = project(M0[0:Q, 0:D], lambda k: o2T[:, k, :], lambda k: wo[l][:, k, :])
                    elif j == "XT":
                        pe.wait_ge(s_xn, n + 1)
                        last = transposes(M1, xn, Q, D)
                    elif j == "Q":
                        pe.wait_ge(s_wq[l], WQ_IN)
                        pe.wait_ge(ev["XT"], n + 1)
                        for m in range(KD):
                            last = project(M0[:, m * Q:(m + 1) * Q], lambda k: wq[l][:, k, m * P:(m + 1) * P], lambda k: xnT[:, k, :])
                    elif j in ("K0", "K1"):
                        m = int(j[1])
                        pe.wait_ge(s_ctx[u], ctx_count(n, u))
                        last = project((M0, M1)[m][:, 0:S], lambda k: wk[l][:, k, m * P:(m + 1) * P], lambda k: ctxT[:, u, k, :])
                    elif j in ("V01", "V2"):
                        dst = M0 if j == "V01" else M1
                        pe.wait_ge(s_ctx[u], ctx_count(n, u))
                        for t in ((0, 1) if j == "V01" else (2,)):
                            last = project(dst[0:SP_, t % 2 * D:(t % 2 + 1) * D], lambda k: ctxT[:, u, k, t * SP_:(t + 1) * SP_], lambda k: wv[l][:, k, :])
                    elif j == "XT2":
                        pe.wait_ge(s_xn2, n + 1)
                        last = transposes(M1, xn2[:, u], Q, D)
                    elif j == "LG":
                        pe.wait_ge(ev["XT2"], n + 1)
                        last = project(M1[0:Q, 0:L.E], lambda k: xn2T[:, k, :], lambda k: rw[l][:, k, :])
                    elif j == "RK":
                        pe.wait_ge(s_sel, n + 1)
                        pe.matmul(M1[0:Q, 0:L.E], con[0:Q, C_TRI:C_TRI + Q], sel[:, 0:L.E], start=True, stop=True)
                        last = pe.matmul(M1[:, L.E:2 * L.E], ones[:, :], sel[:, 0:L.E], start=True, stop=True)
                    last.then_inc(mm[j], 1)

                def ctx_count(n, u):
                    return (n - u) * 16 + 32

                def scores(n, u, h):
                    if h == 0:
                        pe.wait_ge(s_qblk, n + 1)
                        pe.wait_ge(ev["K0"], n + 1)
                    elif h == HPC:
                        pe.wait_ge(ev["K1"], n + 1)
                    before = h - 3 if h >= 3 else h - 4
                    if h < NH - 1:
                        wait(pe, s_ttr, n * NH + (before + 1))
                    m, j = h // HPC, h % HPC
                    pe.matmul(bank[score_bank(h)][0:Q, 0:S], qblk[:, u, m, j, :], kT[:, u, m, :], start=True, stop=True).then_inc(s_sc, 1)

                def probs_T(h, g):
                    pe.wait_ge(s_exp, g + 1)
                    wait(pe, s_tev, g - 1)
                    for t in range(ST):
                        last = pe.transpose(bank[3 + h % 2][0:SP_, t * Q:(t + 1) * Q], xs[:, h % NX, t * SP_:(t + 1) * SP_], ident[0:Q, 0:Q])
                    last.then_inc(s_t, 1)

                def pv(n, u, h):
                    pe.wait_ge(s_tev, n * NH + (h + 1))
                    if h == 0:
                        pe.wait_ge(ev["V01"], n + 1)
                        pe.wait_ge(ev["V2"], n + 1)
                        wait(pe, s_oev, n)
                    for t in range(ST):
                        last = pe.matmul(bank[5][32 * (h % 4):32 * (h % 4) + DH, h // 4 * Q:(h // 4 + 1) * Q], vv[:, u, t, h * DH:(h + 1) * DH],
                                         pT[:, h % 2, t * Q:(t + 1) * Q], start=(t == 0), stop=(t == ST - 1), tile_position=(0, 32 * (h % 4)))
                    last.then_inc(s_pv, 1)

                def first():
                    pe.wait_ge(s_wkv[l], WKV_IN)
                    if l:
                        pe.wait_ge(s_ye, L0.tiles)
                    n = base
                    for j, prev in (("K0", []), ("K1", []), ("XT", [(ev["K1"], n + 1)]), ("V2", [(ev["XT"], n + 1)]), ("V01", [(ev["K0"], n + 1)]),
                                    ("Q", [(ev["V01"], n + 1)])):
                        job(j, n, 0, prev)
                    for h in range(AHEAD_S):
                        scores(n, 0, h)
                    pe.wait_ge(s_wts[l], REST_IN[l])

                def body(n, b, u):
                    free = [[(ev["V01"], n + 1)], [(ev["LG"], n - 1)]]
                    if not in_layer(b, -1):
                        free = [[(ev["Q"], n + 1)], [(ev["V2"], n + 1)]]
                    elif not in_layer(b, -2):
                        free[1] = [(ev["K1"], n + 1)]
                    for h in range(NH):
                        if h < NH - AHEAD_S:
                            if h + AHEAD_S == NH - 1:
                                for sm, v in free[0]:
                                    wait(pe, sm, v)
                                free[0] = [(s_ttr, n * NH + NH)]
                            scores(n, u, h + AHEAD_S)
                        elif in_layer(b, 1):
                            scores(n + 1, 1 - u, h + AHEAD_S - NH)
                        probs_T(h, n * NH + h)
                        for j, at_h in STEP.items():
                            if at_h == h and in_layer(b, ROW[j]):
                                m = 0 if j in BANK_JOBS[0] else 1
                                r = ROW[j]
                                job(j, n + r, (u + r) % 2, free[m])
                                free[m] = [(ev[j], n + (r + 1))]
                        if h >= 2:
                            pv(n, u, h - 2)
                        elif in_layer(b, -1):
                            pv(n - 1, 1 - u, NH - 2 + h)

                def last():
                    n = base + B - 1
                    pv(n, 1, NH - 2)
                    pv(n, 1, NH - 1)
                    job("RK", n - 1, 0, [(ev["LG"], n)])
                    job("OT", n, 1, [(s_ttr, (n + 1) * NH)])
                    job("O2T", n, 1, [(ev["RK"], n)])
                    job("OP", n, 1, [(ev["OT"], n + 1)])
                    job("XT2", n, 1, [(ev["O2T"], n + 1)])
                    job("LG", n, 1, [(ev["XT2"], n + 1)])
                    job("RK", n, 1, [(ev["LG"], n + 1)])

                bodies(pe, L, body, first, last)

            def shared():
                pe.wait_ge(s_swts, 2 * 16)
                pe.wait_ge(s_xall, B + 1)
                pe.wait_ge(ev["RK"], B)
                with pe.Fori(0, 4) as i:
                    for m in range(KD):
                        pe.wait_ge(s_sh, i * 2 + (m + SH_CREDIT - 1))
                        for j in range(2):
                            last = project(bank[2 * m + j][:, 0:4 * Q], lambda k: swu[:, j, k, m * P:(m + 1) * P], lambda k: xnTall[:, k, bass.ds(i * (4 * Q), 4 * Q)])
                        last.then_inc(s_sgu, 1)
                    for r in range(4):
                        if r == 0:
                            pe.wait_ge(s_sh, i * 2 + (2 + SH_CREDIT))
                        pe.wait_ge(s_sev, i * 4 + (r - 1 + SEV_CREDIT))
                        project(bank[4 + r % 2][0:Q, 0:D], lambda k: hh[:, k, r * Q:(r + 1) * Q], lambda k: swd[:, k, :]).then_inc(s_sdn, 1)

            def experts(L):
                l = L.number
                t0 = sum(M.tiles for M in LAYERS[:l])
                pe.wait_ge(s_tabi, 16 * (l + 1))

                def xt(t, u):
                    pe.wait_ge(s_xl[u], x_count(t, u))
                    wait(pe, s_txe, t if l else t - 1)
                    for k in range(KD):
                        last = pe.transpose(xt_bank(u)[:, k * P:(k + 1) * P], xb[:, u, k * P:(k + 1) * P], ident)
                    last.then_inc(s_txt, 1)

                def x_count(t, u):
                    return (t - u) * 4 + 16

                def xt_bank(u):
                    return bank[2 + u % 2] if l == 0 else bank[4]

                def column(tl):
                    return pe.value_load(tabr[0:1, 1, bass.ds(tl, 1)], min_val=0, max_val=(L.ring - 1) * L.cols)

                def gate_up(t, u, col):
                    pe.wait_ge(s_txe, t + 1)
                    if l == 0:
                        wait(pe, s_h, t - 1)
                    wcol = ringbuf
                    if l == 0:
                        for k in range(KD):
                            last = pe.matmul(bank[u % 2][:, 0:2 * L.I], xT[:, u % 2, k, :], wcol[:, bass.ds(col + k * 2 * L.I, 2 * L.I)], start=(k == 0), stop=(k == KD - 1))
                        last.then_inc(s_gu, 1)
                    else:
                        half = L.I // 2
                        for c in range(2):
                            pe.wait_ge(s_h, (t - t0) * 2 + (L0.tiles - 1 + c))
                            for j in range(2):
                                for k in range(KD):
                                    last = pe.matmul(bank[2 * c + j][:, 0:half], xT[:, u % 2, k, :], wcol[:, bass.ds(col + (j * KD + k) * L.I + c * half, half)],
                                                     start=(k == 0), stop=(k == KD - 1))
                            last.then_inc(s_gu, 1)

                def h_T(t, u):
                    if l == 0:
                        pe.wait_ge(s_h, t + 1)
                        wait(pe, s_hte, t - 1)
                        pe.transpose(bank[4 + u % 2][:, 0:P], hh[:, u % 2, 0:P], ident).then_inc(s_ht, 1)
                    else:
                        pe.wait_ge(s_h, (t - t0) * 2 + (L0.tiles + 2))
                        wait(pe, s_hte, t)
                        for c, w in enumerate(L.chunks):
                            last = pe.transpose(bank[5 + c // 4][0:w, c % 4 * P:(c % 4 + 1) * P], hh[:, 0, c * P:c * P + w], ident)
                        last.then_inc(s_ht, 1)

                def down(t, u, col):
                    pe.wait_ge(s_hte, t + 1)
                    wait(pe, s_ye, t - 1 if l == 0 else t)
                    wcol = ringbuf
                    y = bank[6 + u % 2] if l == 0 else bank[7]
                    for c, w in enumerate(L.chunks):
                        last = pe.matmul(y[:, 0:D], hT[0:w, u % 2, c * P:(c + 1) * P], wcol[0:w, bass.ds(col + 2 * L.up + c * D, D)],
                                         start=(c == 0), stop=(c == len(L.chunks) - 1))
                    last.then_inc(s_dn, 1)

                n = L.tiles

                def body(t, tl, u, cols, ahead1, ahead2, behind):
                    if l:
                        if behind:
                            down(t - 1, (u - 1) % 4, cols[-1])
                        if ahead1:
                            xt(t + 1, (u + 1) % 4)
                        h_T(t, u)
                    if ahead1:
                        gate_up(t + 1, (u + 1) % 4, cols[1])
                    nxt = column(tl + 2) if ahead2 else None
                    if l == 0:
                        if ahead2:
                            xt(t + 2, (u + 2) % 4)
                        if behind:
                            down(t - 1, (u - 1) % 4, cols[-1])
                        h_T(t, u)
                    return {-1: cols[0], 0: cols.get(1), 1: nxt}

                xt(t0, 0)
                if l == 0:
                    xt(t0 + 1, 1)
                cols = {0: column(0), 1: column(1)}
                gate_up(t0, 0, cols[0])
                for u in range(4):
                    cols = body(t0 + u, u, u, cols, True, True, u > 0)
                with pe.Fori(0, n // 4 - 2) as i:
                    cols = {k: column(i * 4 + (4 + k)) for k in (-1, 0, 1)}
                    for u in range(4):
                        cols = body(i * 4 + (t0 + 4 + u), i * 4 + (4 + u), u, cols, True, True, True)
                cols = {k: column(n - 4 + k) for k in (-1, 0, 1)}
                for u in range(4):
                    cols = body(t0 + n - 4 + u, n - 4 + u, u, cols, u < 3, u < 2, True)
                down(t0 + n - 1, 3, cols[-1])

            pe.sem_inc(s_dn, 1)
            pe.sem_inc(s_sdn, SDN_CREDIT)
            attention(L0)
            shared()
            pe.wait_ge(s_sev, B + SEV_CREDIT)
            experts(L0)
            attention(L1)
            pe.wait_ge(ev["RK"], 2 * B)
            experts(L1)

        @block.vector
        def _(dve):
            chain = {"base": 0, "n": 0}
            SPAN = 112

            def link(ins):
                chain["n"] += 1
                ins.then_inc(s_dv, 1)
                dve.wait_ge(s_dv, chain["base"] + chain["n"])

            def close():
                assert chain["n"] <= SPAN, chain["n"]
                if chain["n"] < SPAN:
                    dve.sem_inc(s_dv, SPAN - chain["n"])
                chain["n"] = 0

            def start(base):
                chain["base"], chain["n"] = base * SPAN, 0

            dve.memset(ones[:, :], 1.0).then_inc(s_ms, 1)
            dve.memset(zrow[:, :], 0.0).then_inc(s_ms, 1)
            dve.memset(bank[5][:, :], 0.0).then_inc(s_ms, 1)
            dve.memset(yidx_all[:, :, :], 0).then_inc(s_ms, 1)
            dve.sem_inc(s_sh, SH_CREDIT)
            dve.sem_inc(s_sev, SEV_CREDIT)
            dve.wait_ge(s_con, 32)
            dve.wait_ge(s_x, 16)
            dve.tensor_scalar(taun[:, :], tau[:, :], -0.25, None, ALU.mult).then_inc(s_taun, 1)
            dve.wait_ge(s_taun, 1)

            def moments(j, src):
                link(dve.bn_stats(st6[:, :], src))
                hold(dve)
                link(dve.bn_aggr(mv[:, j, :], st6[:, :]))
                dve.sem_inc(s_var[j], 1)

            def norm(j, n, dst, src, signal):
                dve.wait_ge(s_rstd[j], n + 1)
                link(dve.tensor_scalar(dst, src, mv[:, j, 0:1], rstd[:, j:j + 1], ALU.subtract, ALU.mult))
                dve.sem_inc(signal, 1)

            def combine(m, b, u, count, final, part=0, parts=1):
                K = LAYERS[m].K
                if part == 0:
                    dve.wait_ge(s_gat[u], count)
                for k in range(K * part // parts, K * (part + 1) // parts):
                    dst = at(resid, b)
                    if final and k == K - 1:
                        wait(dve, s_out[u], (b - u) * 8)
                        dst = fin[:, u, :]
                    link(dve.scalar_tensor_tensor(dst, yg[:, u, k, :], at(w8[m], b)[:, k:k + 1], at(resid, b), ALU.mult, ALU.add))
                if part == parts - 1:
                    dve.sem_inc(s_cmb, 1)

            def attention(L):
                l, E, K = L.number, L.E, L.K
                base = B * l

                def ttr(n, u, h, g):
                    dve.wait_ge(s_sc, g + 1)
                    if h == 0:
                        dve.wait_ge(s_dl, n + 1)
                    wait(dve, s_t, g - NX + 1)
                    hold(dve)
                    dve.tensor_tensor_reduce(xs[:, h % NX, :], bank[score_bank(h)][0:Q, 0:S], dl[:, u, :], 1.0, BIG, ALU.add, ALU.min, smin[:, h % NX:h % NX + 1]).then_inc(s_ttr, 1)

                def job(j, n, b, u):
                    if j in mm:
                        dve.wait_ge(mm[j], n + 1)
                    if j == "OT":
                        link(dve.reciprocal(rinv[:, :], rs[:, u, :]))
                        link(dve.tensor_tensor(o2[:, :].rearrange("p (h d) -> p h d", h=NH), bank[6][0:Q, :].rearrange("p (h d) -> p h d", h=NH)[:, :, 0:DH],
                                               rinv[:, :].unsqueeze(2).to_broadcast([Q, NH, DH]), ALU.mult))
                        link(dve.tensor_tensor(o2[:, :], o2[:, :], bvo[l][:, 0, :], ALU.add))
                    elif j == "OP":
                        link(dve.tensor_tensor(at(resid, b), at(resid, b), bvo[l][:, 1, :], ALU.add))
                        link(dve.tensor_tensor(at(resid, b), bank[6][0:Q, 0:D], at(resid, b), ALU.add))
                        dve.sem_inc(ev[j], 1)
                        moments(1, at(resid, b))
                        return
                    elif j == "LN2":
                        wait(dve, s_free, n - 1 + FREE_CREDIT)
                        norm(1, n, xn2[:, u, :], at(resid, b), s_xn2)
                        return
                    elif j == "Q":
                        wait(dve, s_qblk, n)
                        for m in range(KD):
                            link(dve.tensor_scalar(qT[:, m, :], bank[6][:, m * Q:(m + 1) * Q], bqk[l][:, 0, m:m + 1], taun[:, bass.ds(b, 1)], ALU.add, ALU.mult))
                    elif j == "RK":
                        link(dve.tensor_tensor(key[:, 0:E], bank[7][0:Q, 0:E], run[0:Q, 0:E], ALU.add))
                        link(dve.tensor_tensor(key[:, 0:E], key[:, 0:E], sel[:, 0:E], ALU.mult))
                        link(dve.tensor_tensor(run[:, 0:E], bank[7][:, E:2 * E], run[:, 0:E], ALU.add))
                    elif j == "SLOT":
                        link(dve.tensor_copy(at(keys[l], b), key[:, 0:E]))
                        hold(dve)
                        link(dve.max(p8[:, :], key[:, 0:E]))
                        wait(dve, s_free, n - 1 + FREE_CREDIT)
                        link(dve.tensor_scalar(idx[:, u, :], p8[:, :], -1.0, None, ALU.add))
                        dve.sem_inc(s_idx, 1)
                        return
                    elif j == "W8":
                        link(dve.tensor_tensor(eq[:, 0:K, 0:E], key[:, 0:E].unsqueeze(1).to_broadcast([Q, K, E]), p8[:, 0:K].unsqueeze(2).to_broadcast([Q, K, E]), ALU.is_equal))
                        link(dve.tensor_tensor(eq[:, 0:K, 0:E], eq[:, 0:K, 0:E], coef[:, 0:E].unsqueeze(1).to_broadcast([Q, K, E]), ALU.mult))
                        link(dve.tensor_reduce(at(w8[l], b), eq[:, 0:K, 0:E], AX.X, ALU.add))
                        return
                    dve.sem_inc(ev[j], 1)

                def top_of_8(values, count):
                    a3 = values.unsqueeze(1).to_broadcast([Q, 8, 8])
                    b3 = values.unsqueeze(2).to_broadcast([Q, 8, 8])
                    link(dve.tensor_tensor(cmpa[:, :, :], a3, b3, ALU.is_gt))
                    link(dve.tensor_tensor(cmpb[:, :, :], a3, b3, ALU.is_equal))
                    link(dve.tensor_tensor(cmpb[:, :, :], cmpb[:, :, :], con[0:Q, C_LT:C_LT + 64].rearrange("p (j i) -> p j i", j=8), ALU.mult))
                    link(dve.tensor_tensor(cmpa[:, :, :], cmpa[:, :, :], cmpb[:, :, :], ALU.add))
                    link(dve.tensor_reduce(rank8[:, :], cmpa[:, :, :], AX.X, ALU.add))
                    link(dve.tensor_scalar(keep8[:, :], rank8[:, :], count - 0.5, None, ALU.is_lt))

                def route(part, n):
                    if l == 0 and part == 0:
                        dve.wait_ge(s_lgx, n + 1)
                        link(dve.tensor_scalar(sc[:, :], sg[:, :], 1.0, None, ALU.add))
                        link(dve.reciprocal(sc[:, :], sc[:, :]))
                        link(dve.tensor_tensor(sfc[:, :], sc[:, :], ebias[:, :], ALU.add))
                        hold(dve)
                        for g in range(8):
                            ins = dve.max(g8[:, g, :], sfc[:, g * 8:(g + 1) * 8])
                        link(ins)
                        link(dve.tensor_tensor(gs[:, :], g8[:, :, 0], g8[:, :, 1], ALU.add))
                    elif l == 0 and part == 1:
                        top_of_8(gs[:, :], 4)
                    elif l == 0 and part == 2:
                        link(dve.tensor_tensor(msk[:, :].rearrange("p (g e) -> p g e", g=8), sfc[:, :].rearrange("p (g e) -> p g e", g=8),
                                               keep8[:, :].unsqueeze(2).to_broadcast([Q, 8, 8]), ALU.mult))
                        hold(dve)
                        link(dve.max(m8[:, :], msk[:, :]))
                        hold(dve)
                        link(dve.match_replace(rep[:, :], m8[:, :], msk[:, :], -BIG))
                        link(dve.tensor_tensor(sel[:, :], rep[:, :], msk[:, :], ALU.not_equal))
                        dve.sem_inc(s_sel, 1)
                    elif l == 0 and part == 3:
                        link(dve.tensor_tensor(wsel[:, :], sc[:, :], sel[:, :], ALU.mult))
                        link(dve.tensor_reduce(wsum[:, :], wsel[:, :], AX.X, ALU.add))
                        link(dve.tensor_scalar(wsum[:, :], wsum[:, :], 1e-20, None, ALU.add))
                        link(dve.reciprocal(winv[:, :], wsum[:, :]))
                        link(dve.tensor_scalar(coef[:, :], wsel[:, :], winv[:, 0:1], 2.5, ALU.mult, ALU.mult))
                    elif part == 0:
                        dve.wait_ge(mm["LG"], n + 1)
                        link(dve.tensor_reduce(wsum[:, :], bank[7][0:Q, 0:E], AX.X, ALU.max))
                        link(dve.tensor_scalar(sc[:, 0:E], bank[7][0:Q, 0:E], wsum[:, 0:1], None, ALU.subtract))
                        dve.sem_inc(ev["LG"], 1)
                        dve.sem_inc(s_pl, 1)
                    elif part == 1:
                        dve.wait_ge(s_lgx, n + 1)
                        link(dve.tensor_reduce(wsum[:, :], sg[:, 0:E], AX.X, ALU.add))
                        link(dve.reciprocal(winv[:, :], wsum[:, :]))
                        link(dve.tensor_scalar(sc[:, 0:E], sg[:, 0:E], winv[:, 0:1], None, ALU.mult))
                    elif part == 2:
                        top_of_8(sc[:, 0:E], K)
                        link(dve.tensor_copy(sel[:, 0:E], keep8[:, :]))
                        dve.sem_inc(s_sel, 1)
                    elif part == 3:
                        link(dve.tensor_tensor(wsel[:, 0:E], sc[:, 0:E], sel[:, 0:E], ALU.mult))
                        link(dve.tensor_reduce(wsum[:, :], wsel[:, 0:E], AX.X, ALU.add))
                        link(dve.tensor_scalar(wsum[:, :], wsum[:, :], 1e-20, None, ALU.add))
                        link(dve.reciprocal(winv[:, :], wsum[:, :]))
                        link(dve.tensor_scalar(coef[:, 0:E], wsel[:, 0:E], winv[:, 0:1], None, ALU.mult))

                if l == 0:
                    EXTRA = {0: [("R0", -2)], 1: [("R1", -2)], 2: [("R2", -2)], 3: [("Q", 1)], 4: [("R3", -2)], 5: [("OT", -1), ("RK", -2)], 6: [("SLOT", -2)],
                             7: [("W8", -2)], 9: [("OP", -1)], 11: [("LN2", -1)], 12: [("MOM", 2)], 15: [("LN1", 2)]}
                else:
                    EXTRA = {0: [("R1", -2)], 1: [("R2", -2)], 3: [("Q", 1)], 4: [("R3", -2)], 5: [("OT", -1), ("RK", -2)], 6: [("SLOT", -2)],
                             7: [("W8", -2), ("C0", 2)], 8: [("C1", 2)], 9: [("OP", -1)], 10: [("C2", 2)], 11: [("LN2", -1)], 12: [("C3", 2)], 13: [("MOM", 2)],
                             15: [("R0", -1), ("LN1", 2)]}

                def extra(j, n, b, u):
                    if j[0] == "R" and j[1].isdigit():
                        route(int(j[1]), n)
                    elif j[0] == "C":
                        combine(0, b, u, (b - u) * (8 * L0.K) + 16 * L0.K, False, int(j[1]), 4)
                    elif j == "MOM":
                        moments(0, at(resid, b))
                    elif j == "LN1":
                        wait(dve, mm["XT"], n)
                        norm(0, n, xn[:, :], at(resid, b), s_xn)
                    else:
                        job(j, n, b, u)

                def first():
                    start(SP_ATTN[l])
                    c = C_R1 if l else C_R0
                    link(dve.tensor_copy(run[:, 0:E], con[:, c:c + E]))
                    for b in range(2):
                        n = base + b
                        if l:
                            for part in range(4):
                                extra(f"C{part}", n, b, b)
                        extra("MOM", n, b, b)
                        extra("LN1", n, b, b)
                        if b == 0:
                            job("Q", n, 0, 0)
                    for h in range(AHEAD_X):
                        ttr(base, 0, h, base * NH + h)
                    dve.wait_ge(s_wts[l], REST_IN[l])
                    close()

                def body(n, b, u):
                    start(b + (SP_ATTN[l] + 1))
                    for h in range(NH):
                        if h < NH - AHEAD_X:
                            ttr(n, u, h + AHEAD_X, n * NH + (h + AHEAD_X))
                        elif in_layer(b, 1):
                            ttr(n + 1, 1 - u, h + AHEAD_X - NH, n * NH + (h + AHEAD_X))
                        for j, r in EXTRA.get(h, ()):
                            if in_layer(b, r):
                                extra(j, n + r, b + r, (u + r) % 2)
                    close()

                def last():
                    n, b = base + B - 1, B - 1
                    start(SP_ATTN[l] + 17)
                    for j in ("R0", "R1", "R2", "R3", "RK", "SLOT", "W8"):
                        if not (l and j == "R0"):
                            extra(j, n - 1, b - 1, 0)
                    for j in ("OT", "OP", "LN2", "R0", "R1", "R2", "R3", "RK", "SLOT", "W8"):
                        extra(j, n, b, 1)
                    close()

                bodies(dve, L, body, first, last)

            def tables(L):
                l, E, K, R = L.number, L.E, L.K, float(L.region)
                start(SP_TAB[l])
                c = C_R1 if l else C_R0
                link(dve.tensor_tensor(cnt[:, 0:E], run[:, 0:E], con[:, c:c + E], ALU.subtract))

                def whole(t):
                    link(dve.tensor_scalar(t, t, 12582912.0, None, ALU.add))
                    link(dve.tensor_scalar(t, t, -12582912.0, None, ALU.add))
                link(dve.tensor_scalar(ntile[:, 0:E], cnt[:, 0:E], 127.0 - 63.5, 1.0 / P, ALU.add, ALU.mult))
                whole(ntile[:, 0:E])
                if L.all_used:
                    link(dve.tensor_scalar(ntile[:, 0:E], ntile[:, 0:E], 1.0, None, ALU.max))
                link(dve.tensor_scalar(act[:, 0:E], ntile[:, 0:E], 0.5, None, ALU.is_gt))
                link(dve.scalar_tensor_tensor(cumA[:, 0:E], act[:, 0:E], 1024.0, ntile[:, 0:E], ALU.mult, ALU.add))
                src, dst, step = cumA, cumB, 1
                while step < E:
                    link(dve.tensor_copy(dst[:, 0:step], src[:, 0:step]))
                    link(dve.tensor_tensor(dst[:, step:E], src[:, step:E], src[:, 0:E - step], ALU.add))
                    src, dst, step = dst, src, step * 2
                link(dve.tensor_scalar(arank[:, 0:E], src[:, 0:E], -511.5, 1.0 / 1024, ALU.add, ALU.mult))
                whole(arank[:, 0:E])
                link(dve.scalar_tensor_tensor(cumt[:, 0:E], arank[:, 0:E], -1024.0, src[:, 0:E], ALU.mult, ALU.add))
                link(dve.scalar_tensor_tensor(back[:, 0:E], cumt[:, 0:E], float(P), run[:, 0:E], ALU.mult, ALU.subtract))
                link(dve.tensor_scalar(back[:, 0:E], back[:, 0:E], 1.0, None, ALU.add))
                total, last_active = cumt[:, E - 1:E], arank[:, E - 1:E]
                for j in range(2):
                    link(dve.tensor_scalar(le[:, 0:E], cumt[:, 0:E], con[:, C_T + j:C_T + j + 1], None, ALU.is_le))
                    link(dve.tensor_reduce(et[:, j:j + 1], le[:, 0:E], AX.X, ALU.add))
                    link(dve.tensor_tensor(lt2[:, 0:E], le[:, 0:E], act[:, 0:E], ALU.mult))
                    link(dve.tensor_reduce(et2[:, j:j + 1], lt2[:, 0:E], AX.X, ALU.add))
                    link(dve.scalar_tensor_tensor(lt2[:, 0:E], con[:, C_E:C_E + E], et[:, j:j + 1], back[:, 0:E], ALU.is_equal, ALU.mult))
                    link(dve.tensor_reduce(ex2[:, j:j + 1], lt2[:, 0:E], AX.X, ALU.add))
                link(dve.tensor_scalar(use2[:, :], et[:, :], E - 0.5, None, ALU.is_lt))
                link(dve.scalar_tensor_tensor(ex2[:, :], con[:, C_T:C_T + 2], float(P), ex2[:, :], ALU.mult, ALU.subtract))
                link(dve.tensor_scalar(ex2[:, :], ex2[:, :], -E * R, None, ALU.add))
                link(dve.tensor_tensor(ex2[:, :], ex2[:, :], use2[:, :], ALU.mult))
                link(dve.tensor_scalar(tabc[:, 0, :], ex2[:, :], E * R, None, ALU.add))
                link(dve.tensor_scalar(fix[:, 0:1], last_active, -1.0, None, ALU.add))
                link(dve.tensor_scalar(et2[:, :], et2[:, :], fix[:, 0:1], None, ALU.min))
                link(dve.tensor_scalar(tabc[:, 2, :], et2[:, :], 1.0, None, ALU.add))
                link(dve.tensor_copy(eti[:, :], et2[:, :]))
                link(dve.tensor_scalar(eti[:, :], eti[:, :], L.ring - 1, None, ALU.bitwise_and))
                link(dve.tensor_scalar(tabc[:, 1, :], eti[:, :], float(L.cols), None, ALU.mult))
                link(dve.tensor_copy(tabc[:, 4, 0:1], last_active))
                link(dve.tensor_copy(tabc[:, 4, 1:2], total))
                link(dve.tensor_tensor(arank[:, 0:E], arank[:, 0:E], act[:, 0:E], ALU.subtract))
                link(dve.scalar_tensor_tensor(le[:, 0:E], arank[:, 0:E], con[:, C_T:C_T + 1], act[:, 0:E], ALU.is_equal, ALU.mult))
                link(dve.tensor_tensor(lt2[:, 0:E], le[:, 0:E], con[:, C_E:C_E + E], ALU.mult))
                link(dve.tensor_reduce(load2[:, 0:1], lt2[:, 0:E], AX.X, ALU.add))
                link(dve.tensor_tensor(lt2[:, 0:E], le[:, 0:E], cumt[:, 0:E], ALU.mult))
                link(dve.tensor_reduce(load2[:, 1:2], lt2[:, 0:E], AX.X, ALU.add))
                link(dve.tensor_scalar(fix[:, 0:1], total, -1.0, float(L.tiles), ALU.mult, ALU.add))
                link(dve.tensor_tensor(fix[:, 1:2], load2[:, 1:2], total, ALU.is_equal))
                link(dve.scalar_tensor_tensor(load2[:, 1:2], fix[:, 1:2], fix[:, 0:1], load2[:, 1:2], ALU.mult, ALU.add))
                link(dve.tensor_scalar(load2[:, 1:2], load2[:, 1:2], 1.0, None, ALU.add))
                link(dve.tensor_copy(tabc[:, 3, :], load2[:, :]))
                dve.sem_inc(s_route, 1)
                close()

            def output_rows(L, b):
                l, E = L.number, L.E
                link(dve.scalar_tensor_tensor(kmax[:, 0:E], at(keys[l], b), 0.0, back[0:Q, 0:E], ALU.is_gt, ALU.mult))
                link(dve.tensor_tensor(kmax[:, 0:E], kmax[:, 0:E], at(keys[l], b), ALU.add))
                hold(dve)
                link(dve.max(p8[:, :], kmax[:, 0:E]))
                link(dve.tensor_scalar(at(yidx_all, b), p8[:, :], -1.0, None, ALU.add))

            def shared():
                with dve.Fori(0, 4) as i:
                    chain["base"] = i * SPAN + SP_SHARED * SPAN
                    chain["n"] = 0
                    for m in range(KD):
                        dve.wait_ge(s_ssil, i * 2 + (m + 1))
                        if m == 0:
                            dve.wait_ge(s_sdn, i * 4 + SDN_CREDIT)
                        dve.tensor_tensor(hh[:, m, 0:4 * Q], sgate[:, m, 0:4 * Q], bank[2 * m + 1][:, 0:4 * Q], ALU.mult).then_inc(s_sh, 1)
                    for r in range(4):
                        output_rows(L0, i * 4 + r)
                        dve.wait_ge(s_sdn, i * 4 + (r + 1 + SDN_CREDIT))
                        link(dve.tensor_tensor(at(resid, i * 4 + r), bank[4 + r % 2][0:Q, 0:D], at(resid, i * 4 + r), ALU.add))
                        dve.sem_inc(s_sev, 1)
                    close()
                dve.sem_inc(s_route, 1)

            def experts(L):
                l = L.number
                t0 = sum(M.tiles for M in LAYERS[:l])

                def xT_ev(t, u):
                    dve.wait_ge(s_txt, t + 1)
                    if l == 0:
                        wait(dve, s_gu, t - 1)
                    else:
                        wait(dve, s_gu, (t - t0) * 2 + (GU_END - 2))
                    src = bank[2 + u % 2] if l == 0 else bank[4]
                    dve.tensor_copy(xT[:, u % 2, :, :].rearrange("p k t -> p (k t)"), src[:, 0:D]).then_inc(s_txe, 1)

                def h(t, u):
                    if l == 0:
                        dve.wait_ge(s_sil, t + 1)
                        wait(dve, s_ht, t - 1)
                        dve.tensor_tensor(hh[:, u % 2, 0:L.I], sgate[:, u % 2, 0:L.I], bank[u % 2][:, L.I:2 * L.I], ALU.mult).then_inc(s_h, 1)
                    else:
                        half = L.I // 2
                        for c in range(2):
                            dve.wait_ge(s_sil, (t - t0) * 2 + (GU_END + c + 1))
                            dve.wait_ge(s_ht, t)
                            dve.tensor_tensor(hh[:, 0, c * half:(c + 1) * half], sgate[:, 0, c * half:(c + 1) * half], bank[2 * c + 1][:, 0:half], ALU.mult).then_inc(s_h, 1)

                def hT_ev(t, u):
                    dve.wait_ge(s_ht, t + 1)
                    dve.wait_ge(s_dn, t)
                    dve.tensor_copy(hT[:, u % 2, 0:4 * P], bank[5][:, 0:4 * P])
                    dve.tensor_copy(hT[:, u % 2, 4 * P:5 * P], bank[6][:, 0:P])
                    dve.tensor_copy(hT[0:64, u % 2, 5 * P:6 * P], bank[6][0:64, P:2 * P]).then_inc(s_hte, 1)

                n = L.tiles
                if l == 0:
                    xT_ev(t0, 0)
                    xT_ev(t0 + 1, 1)

                    h(t0, 0)

                    def body(t, u, ahead1, ahead2):
                        if ahead1:
                            h(t + 1, (u + 1) % 4)
                        if ahead2:
                            xT_ev(t + 2, (u + 2) % 4)
                    for u in range(4):
                        body(t0 + u, u, True, True)
                    with dve.Fori(0, n // 4 - 2) as i:
                        for u in range(4):
                            body(i * 4 + (t0 + 4 + u), u, True, True)
                    for u in range(4):
                        body(t0 + n - 4 + u, u, u < 3, u < 2)
                else:
                    xT_ev(t0, 0)

                    def body(t, u, ahead):
                        if ahead:
                            xT_ev(t + 1, (u + 1) % 4)
                        h(t, u)
                        hT_ev(t, u)
                    for u in range(4):
                        body(t0 + u, u, True)
                        start(SP_ROWS + u)
                        for b in range(4 * u, 4 * u + 4):
                            output_rows(L1, b)
                        close()
                    dve.sem_inc(s_route, 1)
                    with dve.Fori(0, n // 4 - 2) as i:
                        for u in range(4):
                            body(i * 4 + (t0 + 4 + u), u, True)
                    for u in range(4):
                        body(t0 + n - 4 + u, u, u < 3)

            GU_END = L0.tiles
            attention(L0)
            tables(L0)
            shared()
            experts(L0)
            attention(L1)
            tables(L1)
            experts(L1)

            def final(b, u):
                start(b + SP_FIN)
                combine(1, b, u, (b - u) * (8 * L1.K) + (16 * L1.K + 8 * L0.K * B), True)
                close()
            final(0, 0)
            final(1, 1)
            with dve.Fori(0, B // 2 - 1) as i:
                final(i * 2 + 2, 0)
                final(i * 2 + 3, 1)

        @block.scalar
        def _(act):
            def attention(L):
                l = L.number
                base = B * l

                def exp(u, h, g):
                    act.wait_ge(s_ttr, g + 1)
                    act.activation(xs[:, h % NX, :], xs[:, h % NX, :], ACT.Exp, bias=smin[:, h % NX:h % NX + 1], scale=-1.0,
                                   accum_out=rs[:, u, h:h + 1]).then_inc(s_exp, 1)

                def probsT_ev(h, g):
                    act.wait_ge(s_t, g + 1)
                    wait(act, s_pv, g - 1)
                    act.activation(pT[:, h % 2, :], bank[3 + h % 2][0:SP_, 0:ST * Q], ACT.Copy).then_inc(s_tev, 1)

                def out_ev(n):
                    act.wait_ge(s_pv, (n + 1) * NH)
                    act.activation(oT4[:, :], bank[5][:, 0:4 * Q], ACT.Copy).then_inc(s_oev, 1)

                def job(j, n, u):
                    if l and j == "LG":
                        act.wait_ge(s_pl, n + (1 - B))
                        act.activation(sg[:, 0:L.E], sc[:, 0:L.E], ACT.Exp).then_inc(s_lgx, 1)
                        return
                    act.wait_ge(mm[j], n + 1)
                    if j == "O2T":
                        act.activation(o2T[:, :, :].rearrange("p k q -> p (k q)"), bank[7][:, 0:KD * Q], ACT.Copy).then_inc(ev[j], 1)
                    elif j == "XT":
                        act.activation(xnT[:, :, :].rearrange("p k q -> p (k q)"), bank[7][:, 0:KD * Q], ACT.Copy).then_inc(ev[j], 1)
                    elif j == "XT2":
                        if l == 0:
                            act.wait_ge(s_xall, n + 1)
                        act.activation(xn2T[:, :, :].rearrange("p k q -> p (k q)"), bank[7][:, 0:KD * Q], ACT.Copy).then_inc(ev[j], 1)
                    elif j in ("K0", "K1"):
                        m = int(j[1])
                        act.activation(kT[:, u, m, :], bank[6 + m][:, 0:S], ACT.Identity, bias=bqk[l][:, 1, m:m + 1]).then_inc(ev[j], 1)
                    elif j == "LG":
                        act.activation(sg[:, 0:L.E], bank[7][0:Q, 0:L.E], ACT.Exp, scale=-1.0).then_inc(s_lgx, 1)
                        act.wait_ge(s_lgx, n + 1)
                        act.sem_inc(ev[j], 1)
                    elif j == "V01":
                        act.activation(vv[:, u, 0:2, :].rearrange("p t d -> p (t d)"), bank[6][0:SP_, :], ACT.Copy).then_inc(ev[j], 1)
                    elif j == "V2":
                        act.activation(vv[:, u, 2, :], bank[7][0:SP_, 0:D], ACT.Copy).then_inc(ev[j], 1)

                OWN = ("O2T", "XT", "XT2", "K0", "K1", "LG", "V01", "V2")

                def first():
                    act.wait_ge(s_wkv[l], WKV_IN)
                    for j in ("K0", "K1", "XT", "V2", "V01"):
                        job(j, base, 0)
                    for h in range(AHEAD_E):
                        exp(0, h, base * NH + h)

                def body(n, b, u):
                    for h in range(NH):
                        g = n * NH + h
                        if h < NH - AHEAD_E:
                            exp(u, h + AHEAD_E, g + AHEAD_E)
                        elif in_layer(b, 1):
                            exp(1 - u, h + AHEAD_E - NH, g + AHEAD_E)
                        if h:
                            probsT_ev(h - 1, g - 1)
                        elif in_layer(b, -1):
                            probsT_ev(NH - 1, g - 1)
                        if h == 2 and in_layer(b, -1):
                            out_ev(n - 1)
                        if l and h == 0 and in_layer(b, -2):
                            job("LG", n - 2, u)
                        for j, at_h in STEP.items():
                            if at_h + 1 == h and j in OWN and in_layer(b, ROW[j]) and not (l and j == "LG"):
                                job(j, n + ROW[j], 1 - u)

                def last():
                    n = base + B - 1
                    probsT_ev(NH - 1, n * NH + NH - 1)
                    if l:
                        job("LG", n - 1, 0)
                    out_ev(n)
                    for j in ("O2T", "XT2", "LG"):
                        job(j, n, 1)

                bodies(act, L, body, first, last)

            def shared():
                with act.Fori(0, 4) as i:
                    for m in range(KD):
                        act.wait_ge(s_sgu, i * 2 + (m + 1))
                        act.wait_ge(s_sh, i * 2 + (m - 1 + SH_CREDIT))
                        act.activation(sgate[:, m, 0:4 * Q], bank[2 * m][:, 0:4 * Q], ACT.Silu).then_inc(s_ssil, 1)

            def experts(L):
                l = L.number
                t0 = sum(M.tiles for M in LAYERS[:l])
                n = L.tiles

                def silu(t, u):
                    if l == 0:
                        act.wait_ge(s_gu, t + 1)
                        wait(act, s_h, t - 1)
                        act.activation(sgate[:, u % 2, 0:L.I], bank[u % 2][:, 0:L.I], ACT.Silu).then_inc(s_sil, 1)
                    else:
                        half = L.I // 2
                        for c in range(2):
                            act.wait_ge(s_gu, (t - t0) * 2 + (L0.tiles + c + 1))
                            act.wait_ge(s_h, (t - t0) * 2 + (L0.tiles - 1 + c))
                            act.activation(sgate[:, 0, c * half:(c + 1) * half], bank[2 * c][:, 0:half], ACT.Silu).then_inc(s_sil, 1)

                def hT_ev(t, u):
                    act.wait_ge(s_ht, t + 1)
                    wait(act, s_dn, t)
                    act.activation(hT[:, u % 2, 0:P], bank[4 + u % 2][:, 0:P], ACT.Copy).then_inc(s_hte, 1)

                def y_ev(t, tl, u):
                    act.wait_ge(s_dn, t + 2)
                    wait(act, s_yst[u], (t - u) * 4)
                    y = bank[6 + u % 2] if l == 0 else bank[7]
                    act.activation(yb[:, u, :], y[:, 0:D], ACT.Copy).then_inc(s_ye, 1)
                    act.wait_ge(s_ye, t + 1)
                    act.dma_start(y_d[l][bass.ds(tl * P, P), :], yb[:, u, :]).then_inc(s_yst[u], 16)

                if l == 0:
                    silu(t0, 0)

                def body(t, tl, u, ahead, behind):
                    if l == 0:
                        if ahead:
                            silu(t + 1, (u + 1) % 4)
                        if behind:
                            y_ev(t - 1, tl - 1, (u - 1) % 4)
                        hT_ev(t, u)
                    else:
                        silu(t, u)
                        if behind:
                            y_ev(t - 1, tl - 1, (u - 1) % 4)
                for u in range(4):
                    body(t0 + u, u, u, True, u > 0)
                with act.Fori(0, n // 4 - 2) as i:
                    for u in range(4):
                        body(i * 4 + (t0 + 4 + u), i * 4 + (4 + u), u, True, True)
                for u in range(4):
                    body(t0 + n - 4 + u, n - 4 + u, u, u < 3, True)
                y_ev(t0 + n - 1, n - 1, 3)

            act.wait_ge(s_con, 32)
            attention(L0)
            shared()
            experts(L0)
            attention(L1)
            experts(L1)

        @block.gpsimd
        def _(pool):
            pool.sem_inc(s_free, FREE_CREDIT)
            pool.sem_inc(s_xall, 1)
            pool.wait_ge(s_con, 32)

            def delta(n, u):
                pool.wait_ge(s_ctx[u], (n - u) * 16 + 32)
                wait(pool, s_ttr, (n - 1) * NH)
                hold(pool)
                pool.tensor_scalar(dl[:, u, :], draw[:, u, :], -0.25, None, ALU.mult).then_inc(s_dl, 1)

            def spread_q(n, u):
                pool.wait_ge(ev["Q"], n + 1)
                wait(pool, s_sc, (n - 1) * NH)
                for m in range(KD):
                    last = pool.tensor_tensor(qblk[:, u, m, :, :], qT[:, m:m + 1, :].to_broadcast([P, HPC, Q]),
                                              con[:, C_HEAD:C_HEAD + HPC].unsqueeze(2).to_broadcast([P, HPC, Q]), ALU.mult)
                last.then_inc(s_qblk, 1)

            def keep_xnT(n, b):
                pool.wait_ge(ev["XT2"], n + 1)
                pool.tensor_copy(xnTall[:, :, bass.ds(b * Q, Q)], xn2T[:, :, :]).then_inc(s_xall, 1)

            def deviation(j, n):
                pool.wait_ge(s_var[j], n + 1)
                hold(pool)
                pool.tensor_scalar(veps[:, j:j + 1], mv[:, j, 1:2], EPS, None, ALU.add).then_inc(s_veps[j], 1)
                pool.wait_ge(s_veps[j], n + 1)
                pool.tensor_tensor(rstd[:, j:j + 1], veps[:, j:j + 1], con[0:Q, C_MH:C_MH + 1], ALU.pow).then_inc(s_rstd[j], 1)

            def scatter(L, n, u, part):
                pool.wait_ge(s_idx, n + 1)
                hold(pool)
                for k in range(L.K * part // 4, L.K * (part + 1) // 4):
                    pool.indirect_dma_start(xs_d[L.number], bass.IndirectOffsetOnAxis(ap=idx[:, u, k:k + 1], axis=0), xn2[:, u, :], None).then_inc(s_scat[u], 16)

            def gather(m, b, u, copies):
                wait(pool, s_cmb, copies - 1)
                pool.tensor_copy(yidx[:, u, :], at(yidx_all, b)).then_inc(s_yi, 1)
                pool.wait_ge(s_yi, copies + 1)
                hold(pool)
                for k in range(LAYERS[m].K):
                    pool.indirect_dma_start(yg[:, u, k, :], None, y_d[m], bass.IndirectOffsetOnAxis(ap=yidx[:, u, k:k + 1], axis=0)).then_inc(s_gat[u], 16)

            def attention(L):
                l = L.number
                base = B * l

                def landed(b, u):
                    pool.wait_ge(s_scat[u], (b - u) * (8 * L.K) + 16 * (L.K + (L0.K * B // 2 if l else 0)))
                    pool.sem_inc(s_free, 1)

                def first():
                    delta(base, 0)
                    for b in range(2):
                        if l:
                            gather(0, b, b, b)
                    if L.all_used:
                        for s in range(L.ring):
                            pool.dma_start(ring[l][:, s, :], a[f"we{l}"][s]).then_inc(s_wl[l][s], 16)
                    deviation(0, base)
                    spread_q(base, 0)
                    deviation(0, base + 1)

                def body(n, b, u):
                    def part(p):
                        if in_layer(b, -2):
                            scatter(L, n - 2, u, p)
                    if in_layer(b, 1):
                        delta(n + 1, 1 - u)
                    if l and in_layer(b, 2):
                        gather(0, b + 2, u, b + 2)
                    if in_layer(b, 1):
                        spread_q(n + 1, 1 - u)
                    part(0)
                    part(1)
                    if in_layer(b, -1):
                        deviation(1, n - 1)
                    part(2)
                    if in_layer(b, 2):
                        deviation(0, n + 2)
                    if in_layer(b, -1) and l == 0:
                        keep_xnT(n - 1, b - 1)
                    part(3)
                    if in_layer(b, -2):
                        landed(b - 2, u)

                def last():
                    n = base + B - 1
                    for p in range(4):
                        scatter(L, n - 1, 0, p)
                    deviation(1, n)
                    if l == 0:
                        keep_xnT(n, B - 1)
                    landed(B - 2, 0)
                    for p in range(4):
                        scatter(L, n, 1, p)
                    landed(B - 1, 1)

                bodies(pool, L, body, first, last)

            def experts(L):
                l = L.number
                t0 = sum(M.tiles for M in LAYERS[:l])

                def load(e, s):
                    pool.dma_start(ring[l][:, s, :], a[f"we{l}"][bass.ds(e, 1)].rearrange("o p f -> (o p) f")).then_inc(s_wl[l][s], 16)

                def expert_of(r):
                    return pool.value_load(tabr[0:1, 3, bass.ds(r, 1)], min_val=0, max_val=L.E - 1)

                def loaded(s, count):
                    pool.wait_ge(s_wl[l][s], count)
                    pool.sem_inc(s_wr[l], 1)
                if not L.all_used:
                    pool.wait_ge(s_tabi, 16 * (l + 1))
                    for s in range(L.ring):
                        load(expert_of(s), s)
                for s in range(L.ring):
                    loaded(s, 16)
                pool.wait_ge(s_tabi, 16 * (l + 1))
                lag = 1 if L.ring > 2 else 0
                loads = pool.value_load(tabr[0:1, 4, 0:1], min_val=1, max_val=L.E)

                with pool.Fori(0, L.E // L.ring - 1) as i:
                    for s in range(L.ring):
                        r = i * L.ring + (L.ring + s)
                        with pool.If(r < loads):
                            done = pool.value_load(tabr[0:1, 3, bass.ds(i * L.ring + (TT // 2 + s), 1)], min_val=1, max_val=L.tiles + 1)
                            pool.wait_ge(s_dn, done + t0)
                            load(expert_of(r), s)
                            if not lag:
                                loaded(s, i * 16 + 32)
                        if lag and s:
                            with pool.If(r - 1 < loads):
                                loaded(s - 1, i * 16 + 32)
                    if lag:
                        with pool.If(i * L.ring + (2 * L.ring - 1) < loads):
                            loaded(L.ring - 1, i * 16 + 32)
                pool.wait_ge(s_route, ROWS_READY[l])
                for u in range(4):
                    pool.wait_ge(s_yst[u], (t0 + L.tiles) * 4)

            attention(L0)
            experts(L0)
            attention(L1)
            experts(L1)
            gather(1, 0, 0, B)
            gather(1, 1, 1, B + 1)
            with pool.Fori(0, B // 2 - 1) as i:
                gather(1, i * 2 + 2, 0, i * 2 + (B + 2))
                gather(1, i * 2 + 3, 1, i * 2 + (B + 3))


def chunks_first(w):
    return np.ascontiguousarray(w.reshape(KD, P, -1).transpose(1, 0, 2))


def layout(i):
    i = {k: np.asarray(v) for k, v in i.items()}
    a = {"con": constants(), "x": np.ascontiguousarray(i["x"].transpose(1, 0, 2)), "tau": i["condB_tau"], "delta": i["fside_BxS2_0"]}
    a["ctxT"] = np.ascontiguousarray(i["ctx_1024"].transpose(0, 2, 1).reshape(B, KD, P, S).transpose(0, 2, 1, 3).reshape(B, P, KD * S))
    for l in range(2):
        for n in "qkvo":
            a[f"w{n}{l}"] = chunks_first(i[f"L{l}_xcond_W{n}"].T)
        a[f"bqk{l}"] = np.ascontiguousarray(np.stack([i[f"L{l}_xcond_b{n}"].reshape(KD, P).T for n in "qk"], 1))
        a[f"bv{l}"], a[f"bo{l}"] = i[f"L{l}_xcond_bv"], i[f"L{l}_xcond_bo"]
    a["rw0"] = chunks_first(i["L0_ffn_router_w"].T)
    a["rw1"] = chunks_first(i["L1_ffn_Wg"].T)
    a["ebias"] = i["L0_ffn_e_bias"]
    a["swu"] = np.ascontiguousarray(np.stack([chunks_first(i["L0_ffn_SWg"]), chunks_first(i["L0_ffn_SWu"])], 1))
    a["swd"] = chunks_first(i["L0_ffn_SWd"])
    gu = np.stack([i["L0_ffn_Wg"], i["L0_ffn_Wu"]], 2).reshape(L0.E, KD, P, 2 * L0.I).transpose(0, 2, 1, 3).reshape(L0.E, P, -1)
    a["we0"] = np.ascontiguousarray(np.concatenate([gu, i["L0_ffn_Wd"]], 2))
    up = [i[f"L1_ffn_{n}"].transpose(0, 2, 1).reshape(L1.E, KD, P, L1.I).transpose(0, 2, 1, 3).reshape(L1.E, P, -1) for n in ("W1", "W3")]
    pad = len(L1.chunks) * P - L1.I
    down = np.pad(i["L1_ffn_W2"].transpose(0, 2, 1), ((0, 0), (0, pad), (0, 0))).reshape(L1.E, -1, P, D).transpose(0, 2, 1, 3).reshape(L1.E, P, -1)
    a["we1"] = np.ascontiguousarray(np.concatenate(up + [down], 2))
    return a


def kernel(**inputs):
    import concourse.bacc as bacc
    from concourse.bass_utils import run_bass_kernel_spmd

    nc = bacc.Bacc("TRN2", target_bir_lowering=False, num_devices=1)
    arrays = {f"in_{n}": v for n, v in layout(inputs).items()}
    aps = {n[3:]: nc.dram_tensor(n, v.shape, mybir.dt.from_np(v.dtype), kind="ExternalInput").ap() for n, v in arrays.items()}
    out = nc.dram_tensor("out", (B, Q, D), F32, kind="ExternalOutput").ap()
    build(nc, aps, out)
    r = run_bass_kernel_spmd(nc, [arrays], core_ids=[0])
    return r.results[0]["out"]
```
